# Optimizing a Trainium2 kernel written in Bass

```python
import numpy as np
import jax
import jax.numpy as jnp

def _softmax(x, axis=-1):
    return jax.nn.softmax(x, axis=axis)

def _gelu(x):
    return jax.nn.gelu(x, approximate=True)

def _silu(x):
    return jax.nn.silu(x)

def _sigmoid(x):
    return jax.nn.sigmoid(x)

def _layernorm(x, axis=-1, eps=1e-05):
    m = jnp.mean(x, axis=axis, keepdims=True)
    v = jnp.var(x, axis=axis, keepdims=True)
    return (x - m) / jnp.sqrt(v + eps)

def _scatter_add(tgt, idx, src, axis=0):
    return tgt.at[idx].add(src)

def _segment_sum(src, seg, n):
    return jax.ops.segment_sum(src, seg, n)
kernel_name = 'mk_adaln_d1_jaxref_r8_1c1e16'

def setup_inputs(seed: int=0):
    np.random.seed(seed)
    _w = jnp.asarray

    def _L0_attn_setup():
        import jax, jax.numpy as jnp
        import numpy as np
        import math
        B, S, E = (2, 256, 128)
        H, DC, DR = (16, 32, 128)
        HD = E // H

        def _linear_params(key, din, dout):
            k1, k2 = jax.random.split(key)
            bound = 1.0 / math.sqrt(din)
            w = jax.random.uniform(k1, (din, dout), minval=-bound, maxval=bound, dtype=jnp.float32)
            b = jax.random.uniform(k2, (dout,), minval=-bound, maxval=bound, dtype=jnp.float32)
            return (w, b)

        def _gelu(x):
            return jax.nn.gelu(x, approximate=False)

        def _rope_cos_sin(seq_len, d_rope):
            inv_freq = 1.0 / 10000.0 ** (jnp.arange(0, d_rope, 2, dtype=jnp.float32) / d_rope)
            t = jnp.arange(seq_len, dtype=jnp.float32)
            freqs = t[:, None] * inv_freq[None, :]
            emb = jnp.concatenate([freqs, freqs], axis=-1)
            return (jnp.cos(emb), jnp.sin(emb))

        def _apply_rope(x, cos, sin):
            d = x.shape[-1]
            x1, x2 = (x[..., :d // 2], x[..., d // 2:])
            rot = jnp.concatenate([-x2, x1], axis=-1)
            return x * cos + rot * sin
        key = jax.random.key(seed)
        ks = jax.random.split(key, 10)
        x = jax.random.normal(ks[0], (B, S, E), dtype=jnp.float32)
        wq, bq = _linear_params(ks[1], E, DC)
        wqc, bqc = _linear_params(ks[2], DC, E - DR)
        wqr, bqr = _linear_params(ks[3], E, DR)
        wkv, bkv = _linear_params(ks[4], E, DC)
        wkr, bkr = _linear_params(ks[5], E, DR)
        wkc, bkc = _linear_params(ks[6], DC, E - DR)
        wv, bv = _linear_params(ks[7], DC, E)
        wo, bo = _linear_params(ks[8], E, E)
        return dict(x=x, wq=wq, bq=bq, wqc=wqc, bqc=bqc, wqr=wqr, bqr=bqr, wkv=wkv, bkv=bkv, wkr=wkr, bkr=bkr, wkc=wkc, bkc=bkc, wv=wv, bv=bv, wo=wo, bo=bo)
    _L0_attn_in = _L0_attn_setup()

    def _L0_ffn_setup():
        import jax, jax.numpy as jnp
        import numpy as np
        B, S, D = (2, 64, 128)
        E, K, I = (16, 8, 128)
        I_SH = 128
        ROUTE_SCALE = 2.826
        key = jax.random.key(seed)
        ks = jax.random.split(key, 8)
        s = 0.02
        return {'x': jax.random.normal(ks[0], (B, S, D), dtype=jnp.float32), 'gate_w': jax.random.normal(ks[1], (E, D), dtype=jnp.float32) * s, 'expert_bias': jnp.zeros((E,), dtype=jnp.float32), 'w_gate': jax.random.normal(ks[2], (E, I, D), dtype=jnp.float32) * s, 'w_up': jax.random.normal(ks[3], (E, I, D), dtype=jnp.float32) * s, 'w_down': jax.random.normal(ks[4], (E, D, I), dtype=jnp.float32) * s, 'shared_gate_w': jax.random.normal(ks[5], (I_SH, D), dtype=jnp.float32) * s, 'shared_up_w': jax.random.normal(ks[6], (I_SH, D), dtype=jnp.float32) * s, 'shared_down_w': jax.random.normal(ks[7], (D, I_SH), dtype=jnp.float32) * s}
    _L0_ffn_in = _L0_ffn_setup()
    _L0_c = _w((lambda *s: np.random.randn(*s).astype(np.float32) * 0.05)(8, 128))
    _L0_wmod = _w((lambda *s: np.random.randn(*s).astype(np.float32) * 0.05)(128, 6 * 128) * 128 ** (-0.5))
    _d = {'L0_attn_x': _L0_attn_in['x'], 'L0_attn_wq': _L0_attn_in['wq'], 'L0_attn_bq': _L0_attn_in['bq'], 'L0_attn_wqc': _L0_attn_in['wqc'], 'L0_attn_bqc': _L0_attn_in['bqc'], 'L0_attn_wqr': _L0_attn_in['wqr'], 'L0_attn_bqr': _L0_attn_in['bqr'], 'L0_attn_wkv': _L0_attn_in['wkv'], 'L0_attn_bkv': _L0_attn_in['bkv'], 'L0_attn_wkr': _L0_attn_in['wkr'], 'L0_attn_bkr': _L0_attn_in['bkr'], 'L0_attn_wkc': _L0_attn_in['wkc'], 'L0_attn_bkc': _L0_attn_in['bkc'], 'L0_attn_wv': _L0_attn_in['wv'], 'L0_attn_bv': _L0_attn_in['bv'], 'L0_attn_wo': _L0_attn_in['wo'], 'L0_attn_bo': _L0_attn_in['bo'], 'L0_ffn_gate_w': _L0_ffn_in['gate_w'], 'L0_ffn_expert_bias': _L0_ffn_in['expert_bias'], 'L0_ffn_w_gate': _L0_ffn_in['w_gate'], 'L0_ffn_w_up': _L0_ffn_in['w_up'], 'L0_ffn_w_down': _L0_ffn_in['w_down'], 'L0_ffn_shared_gate_w': _L0_ffn_in['shared_gate_w'], 'L0_ffn_shared_up_w': _L0_ffn_in['shared_up_w'], 'L0_ffn_shared_down_w': _L0_ffn_in['shared_down_w'], 'L0_c': _L0_c, 'L0_wmod': _L0_wmod}
    _x0 = _d['L0_attn_x']
    _d['L0_attn_x'] = jax.random.normal(jax.random.fold_in(jax.random.key(seed), 1), (8, 512, 128), dtype=_x0.dtype)
    del _x0
    return _d

def reference(L0_attn_x, L0_attn_wq, L0_attn_bq, L0_attn_wqc, L0_attn_bqc, L0_attn_wqr, L0_attn_bqr, L0_attn_wkv, L0_attn_bkv, L0_attn_wkr, L0_attn_bkr, L0_attn_wkc, L0_attn_bkc, L0_attn_wv, L0_attn_bv, L0_attn_wo, L0_attn_bo, L0_ffn_gate_w, L0_ffn_expert_bias, L0_ffn_w_gate, L0_ffn_w_up, L0_ffn_w_down, L0_ffn_shared_gate_w, L0_ffn_shared_up_w, L0_ffn_shared_down_w, L0_c, L0_wmod):

    def _L0_attn_ref(x, wq, bq, wqc, bqc, wqr, bqr, wkv, bkv, wkr, bkr, wkc, bkc, wv, bv, wo, bo):
        import jax, jax.numpy as jnp
        import numpy as np
        import math
        B, S, E = (2, 256, 128)
        H, DC, DR = (16, 32, 128)
        HD = E // H

        def _linear_params(key, din, dout):
            k1, k2 = jax.random.split(key)
            bound = 1.0 / math.sqrt(din)
            w = jax.random.uniform(k1, (din, dout), minval=-bound, maxval=bound, dtype=jnp.float32)
            b = jax.random.uniform(k2, (dout,), minval=-bound, maxval=bound, dtype=jnp.float32)
            return (w, b)

        def _gelu(x):
            return jax.nn.gelu(x, approximate=False)

        def _rope_cos_sin(seq_len, d_rope):
            inv_freq = 1.0 / 10000.0 ** (jnp.arange(0, d_rope, 2, dtype=jnp.float32) / d_rope)
            t = jnp.arange(seq_len, dtype=jnp.float32)
            freqs = t[:, None] * inv_freq[None, :]
            emb = jnp.concatenate([freqs, freqs], axis=-1)
            return (jnp.cos(emb), jnp.sin(emb))

        def _apply_rope(x, cos, sin):
            d = x.shape[-1]
            x1, x2 = (x[..., :d // 2], x[..., d // 2:])
            rot = jnp.concatenate([-x2, x1], axis=-1)
            return x * cos + rot * sin
        b, s, _ = x.shape
        cq = _gelu(x @ wq + bq)
        q_c = cq @ wqc + bqc
        q_r = x @ wqr + bqr
        ckv = _gelu(x @ wkv + bkv)
        k_r = x @ wkr + bkr
        k_c = ckv @ wkc + bkc
        v = (ckv @ wv + bv).reshape(b, s, H, HD).transpose(0, 2, 1, 3)
        cos, sin = _rope_cos_sin(s, DR)
        q_r = _apply_rope(q_r, cos, sin)
        k_r = _apply_rope(k_r, cos, sin)
        q = _gelu(jnp.concatenate([q_c, q_r], axis=-1)).reshape(b, s, H, HD).transpose(0, 2, 1, 3)
        k = _gelu(jnp.concatenate([k_c, k_r], axis=-1)).reshape(b, s, H, HD).transpose(0, 2, 1, 3)
        scale = 1.0 / math.sqrt(HD)
        scores = jnp.einsum('bhqd,bhkd->bhqk', q, k) * scale
        causal = jnp.triu(jnp.ones((s, s), dtype=bool), k=1)
        scores = jnp.where(causal[None, None], -jnp.inf, scores)
        attn = jax.nn.softmax(scores, axis=-1)
        out = jnp.einsum('bhqk,bhkd->bhqd', attn, v)
        out = out.transpose(0, 2, 1, 3).reshape(b, s, E)
        return out @ wo + bo

    def _L0_ffn_ref(x, gate_w, expert_bias, w_gate, w_up, w_down, shared_gate_w, shared_up_w, shared_down_w):
        import jax, jax.numpy as jnp
        import numpy as np
        B, S, D = (2, 64, 128)
        E, K, I = (16, 8, 128)
        I_SH = 128
        ROUTE_SCALE = 2.826
        gates = jnp.einsum('bsd,ed->bse', x, gate_w)
        scores = jax.nn.sigmoid(gates.astype(jnp.float32))
        sel_scores = scores + expert_bias
        _, inds = jax.lax.top_k(sel_scores, K)
        selected = jnp.take_along_axis(scores, inds, axis=-1)
        selected = selected / selected.sum(axis=-1, keepdims=True)
        selected = selected * ROUTE_SCALE
        onehot = jax.nn.one_hot(inds, E, dtype=selected.dtype)
        combine = jnp.einsum('bske,bsk->bse', onehot, selected)
        hg = jnp.einsum('bsd,eid->bsei', x, w_gate)
        hu = jnp.einsum('bsd,eid->bsei', x, w_up)
        h = jax.nn.silu(hg) * hu
        ye = jnp.einsum('bsei,edi->bsed', h, w_down)
        y = jnp.einsum('bsed,bse->bsd', ye, combine).astype(x.dtype)
        g = jnp.einsum('bsd,id->bsi', x, shared_gate_w)
        u = jnp.einsum('bsd,id->bsi', x, shared_up_w)
        y = y + jnp.einsum('bsi,di->bsd', jax.nn.silu(g) * u, shared_down_w)
        return y
    x = L0_attn_x
    mod = (_silu(L0_c) @ L0_wmod).reshape(L0_c.shape[0], 6, 1, -1)
    sa, ca, ga, sb, cb, gb = (mod[:, 0], mod[:, 1], mod[:, 2], mod[:, 3], mod[:, 4], mod[:, 5])
    ga = (2 * (ga >= 0) - 1) * jnp.maximum(jnp.abs(ga), 0.25)
    gb = (2 * (gb >= 0) - 1) * jnp.maximum(jnp.abs(gb), 0.25)
    h = _layernorm(x, axis=-1) * (1 + ca) + sa
    x = x + ga * _L0_attn_ref(h, L0_attn_wq, L0_attn_bq, L0_attn_wqc, L0_attn_bqc, L0_attn_wqr, L0_attn_bqr, L0_attn_wkv, L0_attn_bkv, L0_attn_wkr, L0_attn_bkr, L0_attn_wkc, L0_attn_bkc, L0_attn_wv, L0_attn_bv, L0_attn_wo, L0_attn_bo)
    h = _layernorm(x, axis=-1) * (1 + cb) + sb
    x = x + gb * _L0_ffn_ref(h, L0_ffn_gate_w, L0_ffn_expert_bias, L0_ffn_w_gate, L0_ffn_w_up, L0_ffn_w_down, L0_ffn_shared_gate_w, L0_ffn_shared_up_w, L0_ffn_shared_down_w)
    return x

_drawn_inputs = setup_inputs


def setup_inputs(seed=0):
    import zlib

    import numpy as np

    out = dict(_drawn_inputs(seed))
    spreads = {'L0_ffn_expert_bias': (0.0, 0.8)}
    factors = {'L0_attn_wqr': 8.0,
     'L0_attn_bqr': 8.0,
     'L0_attn_wkv': 8.0,
     'L0_attn_bkv': 8.0,
     'L0_attn_wkr': 8.0,
     'L0_attn_bkr': 8.0,
     'L0_attn_wv': 5.761,
     'L0_attn_bv': 3.36,
     'L0_attn_wo': 2.736,
     'L0_attn_bo': 13.888,
     'L0_ffn_gate_w': 8.0,
     'L0_ffn_w_gate': 8.0,
     'L0_ffn_w_up': 8.0,
     'L0_ffn_w_down': 8.0,
     'L0_ffn_shared_gate_w': 8.0,
     'L0_ffn_shared_up_w': 8.0,
     'L0_ffn_shared_down_w': 8.0}
    for name, (base, spread) in spreads.items():
        noise = np.random.default_rng([zlib.crc32(name.encode()), seed]).standard_normal(out[name].shape)
        drawn = base * np.exp(spread * noise) if base else spread * noise
        out[name] = jnp.asarray(drawn.astype(out[name].dtype))
    for name, factor in factors.items():
        out[name] = (out[name] * factor).astype(out[name].dtype)
    return out
```

```python
from contextlib import ExitStack

import concourse.bass as bass
from concourse import mybir

F32 = mybir.dt.float32
BF16 = mybir.dt.bfloat16
F32R = mybir.dt.float32r
I32 = mybir.dt.int32
U32 = mybir.dt.uint32
U16 = mybir.dt.uint16
ALU = mybir.AluOpType
ACT = mybir.ActivationFunctionType
AX = mybir.AxisListType

B, S, E = 8, 512, 128
H, DH = 16, 8
DC = 32
NE, TOPK = 16, 8
NF = NE + 1
P = 128
NT = S // P
PAIRS, QUADS = H // 2, H // 4
EPS = 1e-5
ROUTE_SCALE = 2.826
SCALE = float(DH) ** -0.5
NEG = -3.0e38

Q_PART = (0, 1, 2, 0, 1, 0)
K_PART = (0, 0, 0, 1, 1, 2)
MROW = DH * len(Q_PART)

VW = DH + 1
P_AT = (0, 512, 1024, 896)
PCOLS = 1280
E_SLOT1 = 11
ROW_TILES = 5
ROW_STEPS = range(1, 9)
KEY_ORDER = (0, 1, 3, 2)
LN1_AT = {4: 0, 9: 1, 10: 2}
ATTEND_AT = {5: (0,), 6: (1,), 7: (2,), 8: (3,), 10: (4,), 11: (5, 6, 7), 13: (8,), 14: (9,), 15: (10,)}
GELU_AT = 9


ONES_BF16 = 1.0 + 2.0 ** -9 - 2.0 ** -16


HIGH_BITS = 0xFFFFF000


class Batch:

    def __init__(self, const, reg=None):
        self.const, self.reg = const, reg

    def of(self, per, k):
        v = self.const * per + k
        return v if self.reg is None else self.reg * (2 * per) + v

    def index(self):
        return self.const if self.reg is None else self.reg * 2 + self.const

    def plus(self, n):
        return Batch(self.const + n, self.reg)

    @property
    def par(self):
        return self.const % 2


def wait(eng, sem, batch, per, k):
    v = batch.of(per, k)
    if batch.reg is None and v <= 0:
        return
    assert batch.const * per + k > 0
    eng.wait_ge(sem, v)


def adaln_block(nc, x, cT, wmod, wqkv, bqk, wkv, bkv, wv, wo, bo, trig, gate, ebias, wg, wu, wd,
                ident, mask, out, scratch):
    with ExitStack() as ctx:
        def sb(name, shape, dt=F32):
            return ctx.enter_context(nc.sbuf_tensor(name, shape, dt))

        def sem(name):
            return ctx.enter_context(nc.semaphore(name))

        banks = ctx.enter_context(nc.psum_tensor("banks", [P, 8, 512], F32))

        wqkv_sb = sb("wqkv_sb", [P, 4, P])
        bqk_sb = sb("bqk_sb", [P, 4])
        wkv_sb = sb("wkv_sb", [P, DC])
        bkv_sb = sb("bkv_sb", [DC, 1])
        wv_sb = sb("wv_sb", [DC + 1, P])
        wo_sb = sb("wo_sb", [P, P])
        bo_sb = sb("bo_sb", [P, 1])
        trig_sb = sb("trig_sb", [P, 2, S])
        gate_sb = sb("gate_sb", [P, NE])
        ebias_sb = sb("ebias_sb", [P, NT, NE])
        wg_hi, wg_lo = sb("wg_hi", [P, NF, P], F32R), sb("wg_lo", [P, NF, P], F32R)
        wu_hi, wu_lo = sb("wu_hi", [P, NF, P], F32R), sb("wu_lo", [P, NF, P], F32R)
        wd_sb = sb("wd_sb", [P, NF, P])
        ident_sb = sb("ident_sb", [P, P])
        identb = sb("identb", [P, P], BF16)
        mask_sb = sb("mask_sb", [P, P], BF16)
        c_sb = sb("c_sb", [P, B])
        cs_sb = sb("cs_sb", [P, B])
        sign = sb("sign", [P, 2, B])
        size = sb("size", [P, 2, B])
        root = sb("root", [P, 3, NT])
        mods = sb("mods", [P, B, 7])

        xt = sb("xt", [P, 2, NT, P])
        x1 = sb("x1", [P, 2, NT, P])
        mod_a = sb("mod_a", [P, 2, 7])
        gate_rows = sb("gate_rows", [P, B, E])
        gate_b = sb("gate_b", [P, 2, E])
        stats = sb("stats", [P, NT, 6])
        mv = sb("mv", [P, NT, 2])
        rstd = sb("rstd", [P, NT])
        xn = sb("xn", [P, NT, P])
        hT = sb("hT", [P, S])
        rot = sb("rot", [P, 2, S])
        qk = sb("qk", [P, 2, S])
        rest = sb("rest", [P, S])
        parts = sb("parts", [P, 2, 3, S], BF16)
        qs = sb("qs", [P, H, S], BF16)
        ks = sb("ks", [P, H, S], BF16)
        ckv = sb("ckv", [DC + 1, S])
        vpad = sb("vpad", [P, NT, H, 32])
        mpart = sb("mpart", [P, H, 4])
        idle = sb("idle", [P, 1])
        idle_pool = sb("idle_pool", [P, 1])
        idle_act = sb("idle_act", [P, 1])
        mx = sb("mx", [P, NT, H])
        mrest = sb("mrest", [P, NT, H])
        msplit = sb("msplit", [P, NT, P // H, H], BF16)
        mT = sb("mT", [3 * H, S], BF16)
        probs = sb("probs", [P, 8, PCOLS])
        xs = rot
        rden = sb("rden", [P, 2, NT, 4, 2])
        o = sb("o", [P, NT, P])
        oT = hT
        aT = o[:, :, :].rearrange("p n e -> p (n e)")
        stats2 = sb("stats2", [P, NT, 6])
        mv2 = sb("mv2", [P, NT, 2])
        rstd2 = sb("rstd2", [P, NT])
        h2T = sb("h2T", [P, S])
        h2bits = sb("h2bits", [P, S], U32)
        h2_hi, h2_lo = sb("h2_hi", [P, 2, S], F32R), sb("h2_lo", [P, 2, S], F32R)
        eg = sb("eg", [P, NT, NE])
        eg1 = sb("eg1", [P, NT, NE])
        score = sb("score", [P, NT, NE])
        pick = sb("pick", [P, NT, NE])
        top = sb("top", [P, NT, 8])
        left = sb("left", [P, NT, NE])
        chosen = sb("chosen", [P, NT, NE])
        total = sb("total", [P, NT])
        rtotal = sb("rtotal", [P, NT])
        comb = sb("comb", [P, 2, NT, NE])
        silu = sb("silu", [P, 2, S])
        hid = sb("hid", [P, 2, S])
        ye = sb("ye", [P, 2, S])
        y_sum = sb("y_sum", [P, S])
        wmod_sb = silu[:, :, :].rearrange("p a c -> p (a c)")[:, 0:6 * P].rearrange("p (m e) -> p m e", m=6)
        yo = sb("yo", [P, NT, P])
        staged = probs[:, :, :].rearrange("p h c -> p (h c)")[:, 0:4 * NF * P].rearrange("p (m f e) -> p m f e", m=4, f=NF)

        def row_tile(n):
            return banks[:, n % 4, :]

        def col_pair(h):
            return banks[:, 2 * (h % 2):2 * (h % 2) + 2, :]
        col_shared = banks[:, 4, :]
        b_up = banks[:, 4, :]
        b_gate = banks[:, 5, :]
        b_attn = (banks[:, 5, :], banks[:, 6, :])
        b_values = banks[:, 3, :]

        def b_proj(b, k):
            return banks[:, (6, 0, 1, 2, 4, 5)[k] if b.reg is None and b.const == 0 else 6, :]
        b_y = banks[:, 7, :]

        mod_loaded, w_loaded, late_loaded, ffn_loaded = sem("mod_loaded"), sem("w_loaded"), sem("late_loaded"), sem("ffn_loaded")
        act_setup, pe_setup, dve_setup, pool_setup = sem("act_setup"), sem("pe_setup"), sem("dve_setup"), sem("pool_setup")
        x_loaded = sem("x_loaded")
        dve_ln1 = sem("dve_ln1"); LN1 = 21
        pe_a = sem("pe_a"); PA = 7
        dve_h = sem("dve_h")
        dve_rope = sem("dve_rope")
        pool_rope = sem("pool_rope")
        act_gelu = sem("act_gelu")
        q_split, k_split = sem("q_split"), sem("k_split")
        q_scr, k_scr = sem("q_scr"), sem("k_scr")
        stacks = sem("stacks"); ST = 13 * 16
        dve_v = sem("dve_v")
        pe_rows = sem("pe_rows"); RT = 5 * PAIRS
        dve_rows = sem("dve_rows")
        dve_m = sem("dve_m")
        pe_mT = sem("pe_mT")
        dve_mT = sem("dve_mT")
        m_rows = sem("m_rows")
        pe_cols = sem("pe_cols"); CT = 3 * PAIRS
        act_exp = sem("act_exp")
        pe_pv = sem("pe_pv")
        dve_x = sem("dve_x")
        pe_c = sem("pe_c"); PC = 6
        act_c = sem("act_c"); AC = 5
        dve_bits = sem("dve_bits")
        pool_low = sem("pool_low")
        dve_wsplit, act_wsplit = sem("dve_wsplit"), sem("act_wsplit")
        dve_o = sem("dve_o")
        dve_ln2 = sem("dve_ln2"); LN2 = 22
        dve_g = sem("dve_g"); DG = 15
        pe_gate, pe_up, pe_down = sem("pe_gate"), sem("pe_up"), sem("pe_down")
        act_silu = sem("act_silu")
        dve_hid = sem("dve_hid")
        act_ye = sem("act_ye")
        pool_sum = sem("pool_sum")
        pool_y = sem("pool_y")
        dve_diag, pe_rows_b, act_rows_b = sem("dve_diag"), sem("pe_rows_b"), sem("act_rows_b")
        stored = sem("stored")

        block = ctx.enter_context(nc.Block())

        mod_loads = [(cT, c_sb), (wmod, wmod_sb), (bo, bo_sb)]
        loads = [(ident, ident_sb), (wqkv, wqkv_sb), (bqk, bqk_sb), (trig, trig_sb), (wkv, wkv_sb), (bkv, bkv_sb),
                 (wv, wv_sb)]
        late_loads = [(wo, wo_sb), (gate, gate_sb), (ebias, ebias_sb)]
        ffn_loads = [(wg, staged[:, 0]), (wu, staged[:, 1]), (wd, wd_sb)]
        BODIES = (B - 2) // 2

        def schedule(eng, stage):
            stage(Batch(0), False, True)
            with eng.Fori(0, BODIES) as j:
                for u in (1, 2):
                    stage(Batch(u, j), True, True)
            stage(Batch(B - 1), True, False)

        @block.sync
        def _(sp):
            def load(group, done):
                for src, dst in group:
                    dst = dst[tuple([slice(None)] * len(dst.shape))]
                    if src.dtype == U16:
                        dst = dst.bitcast(U16)
                    sp.dma_start(dst, src).then_inc(done, 16)

            def load_x(b):
                if not (b.reg is None and b.const < 2):
                    wait(sp, dve_ln2, b.plus(-2), LN2, 1)
                src = x[bass.ds(b.index(), 1), :, :].rearrange("b (n p) e -> p (b n) e", p=P)
                sp.dma_start(xt[:, b.par, :, :], src).then_inc(x_loaded, 16)

            def send_stacks(b):
                for t, (scr_sem, part_of, stack, done) in enumerate(
                        ((q_scr, Q_PART, qs, q_split), (k_scr, K_PART, ks, k_split))):
                    wait(sp, done, b, 4, 4)
                    sp.dma_start(scratch[b.par, t], parts[:, t, :, :]).then_inc(scr_sem, 16)
                if not (b.reg is None and b.const == 0):
                    wait(sp, pe_cols, b.plus(-1), CT, CT)
                sp.dma_start(qs[MROW:MROW + 3, :, :], qs[64:67, :, :]).then_inc(stacks, 16)
                for t, (scr_sem, part_of, stack) in enumerate(((q_scr, Q_PART, qs), (k_scr, K_PART, ks))):
                    wait(sp, scr_sem, b, 16, 16)
                    src = scratch[b.par, t].rearrange("(h d) s c -> s d h c", d=DH)
                    for row, s_ in enumerate(part_of):
                        sp.dma_start(stack[DH * row:DH * (row + 1), :, :], src[s_]).then_inc(stacks, 16)

            def stage(i, ffn, proj):
                if proj:
                    load_x(i.plus(1))
                wait(sp, dve_mT, i, 1, 1)
                for s in range(3):
                    sp.dma_start(qs[MROW + s:MROW + s + 1, :, :], mT[s * H:(s + 1) * H, :]).then_inc(m_rows, 16)
                if proj:
                    send_stacks(i.plus(1))
                if ffn:
                    store(i.plus(-1))

            def store(b):
                wait(sp, pool_y, b, 1, 2)
                dst = out[bass.ds(b.index(), 1), :, :].rearrange("b (n p) e -> p (b n) e", p=P)
                sp.dma_start(dst, yo[:, :, :]).then_inc(stored, 16)

            load(mod_loads, mod_loaded)
            load_x(Batch(0))
            load(loads, w_loaded)
            load([(mask, mask_sb)], stored)
            load(late_loads, late_loaded)
            load(ffn_loads, ffn_loaded)
            send_stacks(Batch(0))
            schedule(sp, stage)
            store(Batch(B - 1))
            sp.wait_ge(stored, 16 * (B + 1))
            sp.wait_ge(q_scr, 16 * B)
            sp.wait_ge(k_scr, 16 * B)

        @block.gpsimd
        def _(pool):
            def as_words(t):
                return t.rearrange("p h c -> p (h c)").bitcast(F32)

            pool.memset(as_words(ks[:, :, :]), 0.0).then_inc(pool_setup, 1)
            pool.wait_ge(pool_setup, 1)
            pool.memset(as_words(ks[32:64, :, :]), ONES_BF16).then_inc(pool_setup, 1)
            pool.wait_ge(pool_setup, 2)
            pool.memset(vpad[:, :, :, :], 0.0).then_inc(pool_setup, 1)
            pool.wait_ge(pool_setup, 3)
            for r in range(2):
                v = vpad[:, :, :, :].rearrange("p n (g r c) w -> p (n g) r c w", g=2, r=2)
                pool.memset(v[:, :, r, :, VW * r + DH:VW * r + DH + 1], 1.0).then_inc(pool_setup, 1)
            pool.memset(ckv[:, :], 1.0).then_inc(pool_setup, 1)

            def carry(b):
                if b.reg is not None:
                    pool.tensor_tensor(idle_pool[:, :], bo_sb[:, :], bo_sb[:, :], ALU.add)

            def rope_sum(b, t):
                wait(pool, dve_rope, b, 4, 2 * t + 2)
                if t == 0 and not (b.reg is None and b.const == 0):
                    wait(pool, k_split, b.plus(-1), 4, 4)
                pool.tensor_tensor(qk[:, t, :], rot[:, 0, :], rot[:, 1, :], ALU.add).then_inc(pool_rope, 1)

            def split(b, t):
                wait(pool, act_gelu, b, 3, 3)
                done = (q_split, k_split)[t]
                if not (b.reg is None and b.const == 0):
                    wait(pool, (q_scr, k_scr)[t], b.plus(-1), 16, 16)
                carry(b)
                pool.tensor_copy(parts[:, t, 0, :], qk[:, t, :]).then_inc(done, 1)
                wait(pool, done, b, 4, 1)
                pool.tensor_tensor(rest[:, :], qk[:, t, :], parts[:, t, 0, :], ALU.subtract).then_inc(done, 1)
                wait(pool, done, b, 4, 2)
                carry(b)
                pool.tensor_copy(parts[:, t, 1, :], rest[:, :]).then_inc(done, 1)
                wait(pool, done, b, 4, 3)
                pool.tensor_tensor(parts[:, t, 2, :], rest[:, :], parts[:, t, 1, :], ALU.subtract).then_inc(done, 1)

            def proj_a(b):
                rope_sum(b, 0)
                rope_sum(b, 1)
                split(b, 0)
                if not (b.reg is None and b.const == 0):
                    wait(pool, q_split, b, 4, 4)
                    split(b, 1)

            def low_part(b):
                wait(pool, dve_bits, b, 1, 1)
                pool.tensor_tensor(h2_lo[:, b.par, :], h2T[:, :], h2bits[:, :].bitcast(F32), ALU.subtract).then_inc(pool_low, 1)

            def add(b, e):
                wait(pool, act_ye, b, NF, e + 1)
                if e == 1:
                    wait(pool, pool_y, b, 1, 1)
                    before = ye[:, b.par, :]
                else:
                    wait(pool, pool_sum, b, NF, e - 1)
                    before = y_sum[:, :]
                pool.tensor_tensor(y_sum[:, :], before, ye[:, (b.const + e) % 2, :], ALU.add).then_inc(pool_sum, 1)

            def finish(b):
                wait(pool, pool_sum, b, NF, NF - 1)
                wait(pool, stored, b, 16, 16)
                wait(pool, dve_ln2, b, LN2, 2)
                pool.tensor_tensor(yo[:, :, :], y_sum[:, :].rearrange("p (n e) -> p n e", n=NT),
                                   gate_b[:, b.par:b.par + 1, :].broadcast_to([P, NT, E]), ALU.mult).then_inc(pool_sum, 1)
                wait(pool, pool_sum, b, NF, NF)
                pool.tensor_tensor(yo[:, :, :], yo[:, :, :], x1[:, b.par], ALU.add).then_inc(pool_y, 1)

            def stage(i, ffn, proj):
                prev = i.plus(-1)
                if ffn:
                    for e in range(1, E_SLOT1 - 1):
                        add(prev, e)
                if proj:
                    proj_a(i.plus(1))
                if ffn:
                    for e in range(E_SLOT1 - 1, 15):
                        add(prev, e)
                low_part(i)
                if ffn:
                    add(prev, 15)
                    add(prev, 16)
                    finish(prev)

            pool.wait_ge(w_loaded, 16 * len(loads))
            proj_a(Batch(0))
            pool.wait_ge(act_rows_b, 2)
            pool.memset(idle_pool[:, :], 0.0).then_inc(pool_y, 1)
            pool.wait_ge(pool_y, 1)
            schedule(pool, stage)
            for e in range(1, NF):
                add(Batch(B - 1), e)
            finish(Batch(B - 1))

        @block.scalar
        def _(act):
            act.wait_ge(mod_loaded, 16 * len(mod_loads))
            act.activation(cs_sb[:, :], c_sb[:, :], ACT.Silu).then_inc(act_setup, 1)

            def gelus(b):
                wait(act, pool_rope, b, 2, 2)
                for t in range(2):
                    act.activation(qk[:, t, :], qk[:, t, :], ACT.Gelu).then_inc(act_gelu, 1)
                wait(act, pe_a, b, PA, 6)
                act.activation(ckv[0:DC, :], b_proj(b, 5)[0:DC, :], ACT.Gelu, bias=bkv_sb[:, 0:1]).then_inc(act_gelu, 1)

            def silu_of(b, e):
                wait(act, pe_gate, b, NF, e + 1)
                if e >= 2:
                    wait(act, dve_hid, b, NF, e - 1)
                act.activation(silu[:, (b.const + e) % 2, :], b_gate, ACT.Silu).then_inc(act_silu, 1)

            def exp_pair(i, h):
                n = 3 * (h // 2) + h % 2
                wait(act, pe_cols, i, CT, n + 1)
                free_probs(i, h)
                act.activation(probs[:, h % 8, 0:1024].rearrange("p (a c) -> p a c", a=2), col_pair(h),
                               ACT.Exp, scale=SCALE).then_inc(act_exp, 1)

            def free_probs(i, h):
                if h >= 8:
                    wait(act, pe_pv, i, H, 4 * ((h - 8) // 4 + 1))
                elif not (i.reg is None and i.const == 0):
                    wait(act, pe_pv, i, H, 0)

            def exp_shared(i, h):
                wait(act, pe_cols, i, CT, 3 * (h // 2) + 3)
                act.activation(probs[:, h % 8:h % 8 + 2, 1024:1280],
                               col_shared.rearrange("p (a c) -> p a c", a=2),
                               ACT.Exp, scale=SCALE).then_inc(act_exp, 1)

            def weigh(b, e):
                if e < 2:
                    wait(act, pool_y, b, 1, 1)
                else:
                    wait(act, pool_sum, b, NF, max(e - 2, 1))
                if e == 0:
                    wait(act, dve_g, b, DG, DG)
                wait(act, pe_down, b, NF, e + 1)
                dst = ye[:, (b.const + e) % 2, :]
                if e == NE:
                    act.activation(dst, b_y, ACT.Copy).then_inc(act_ye, 1)
                    return
                for n in range(NT):
                    ins = act.activation(dst[:, n * P:(n + 1) * P], b_y[:, n * P:(n + 1) * P], ACT.Copy,
                                         scale=comb[:, b.par, n, e:e + 1])
                ins.then_inc(act_ye, 1)

            def stage(i, ffn, proj):
                prev, nxt = i.plus(-1), i.plus(1)
                if ffn:
                    silu_of(prev, 0)
                    for e in range(1, E_SLOT1):
                        silu_of(prev, e)
                        if e < E_SLOT1 - 1:
                            weigh(prev, e - 1)
                act.activation(idle_act[:, :], bo_sb[:, :], ACT.Exp)
                for h in range(H):
                    exp_pair(i, h)
                    if h % 2:
                        exp_shared(i, h - 1)
                    if ffn and h == 3:
                        weigh(prev, E_SLOT1 - 2)
                    if proj and h == GELU_AT:
                        gelus(nxt)
                if ffn:
                    weigh(prev, 10)
                    silu_of(prev, 11)
                    silu_of(prev, 12)
                wait(act, pe_c, i, PC, 2)
                act.activation(oT[:, :], banks[:, 2, :], ACT.Copy).then_inc(act_c, 1)
                if ffn:
                    weigh(prev, 11)
                wait(act, pe_c, i, PC, 3)
                act.activation(aT, banks[:, 3, :], ACT.Identity, bias=mod_a[:, i.par, 6:7],
                               scale=mod_a[:, i.par, 2:3]).then_inc(act_c, 1)
                if ffn:
                    silu_of(prev, 13)
                    weigh(prev, 12)
                    silu_of(prev, 14)
                    weigh(prev, 13)
                    silu_of(prev, 15)
                    weigh(prev, 14)
                    silu_of(prev, 16)
                wait(act, pe_c, i, PC, 5)
                if not (i.reg is None and i.const == 0):
                    wait(act, pool_low, prev, 1, 1)
                act.activation(h2T[:, :], banks[:, 1, :], ACT.Identity, bias=mod_a[:, i.par, 3:4],
                               scale=mod_a[:, i.par, 4:5]).then_inc(act_c, 1)
                wait(act, dve_bits, i, 1, 1)
                act.activation(h2_hi[:, i.par, :], h2bits[:, :].bitcast(F32), ACT.Copy).then_inc(act_c, 1)
                if ffn:
                    weigh(prev, 15)
                wait(act, pe_c, i, PC, 6)
                act.activation(eg[:, :, :], banks[:, 2, 0:NT * NE].rearrange("p (n e) -> p n e", n=NT),
                               ACT.Exp, scale=-1.0).then_inc(act_c, 1)
                if ffn:
                    weigh(prev, 16)

            act.wait_ge(w_loaded, 16 * len(loads))
            act.wait_ge(pool_setup, 6)
            gelus(Batch(0))
            act.wait_ge(pe_rows_b, 1)
            for n in range(2):
                act.activation(gate_rows[:, 4 * n:4 * n + 4, :], banks[:, 1 + n, :].rearrange("p (b e) -> p b e", e=E),
                               ACT.Copy).then_inc(act_rows_b, 1)
            act.wait_ge(dve_wsplit, 2)
            for m, dst in enumerate((wg_hi, wu_hi)):
                act.activation(dst[:, :, :], staged[:, 2 + m], ACT.Copy).then_inc(act_wsplit, 1)
            act.wait_ge(dve_wsplit, 4)
            act.wait_ge(act_wsplit, 2)
            schedule(act, stage)
            last = Batch(B - 1)
            silu_of(last, 0)
            for e in range(1, NF):
                silu_of(last, e)
                weigh(last, e - 1)
            weigh(last, NF - 1)

        @block.vector
        def _(dve):
            v = nc.vector
            v.memset(qs[:, :, :].rearrange("p h c -> p (h c)").bitcast(F32), 0.0).then_inc(dve_setup, 1)
            v.memset(msplit[:, :, :, :], 0.0).then_inc(dve_setup, 1)
            v.memset(y_sum[:, 0:P], 1.0).then_inc(dve_setup, 1)
            dve.wait_ge(pe_setup, 1)
            raw = banks[:, 0, 0:6 * B].rearrange("p (m b) -> p m b", m=6)
            for m in (0, 3):
                v.tensor_copy(mods[:, :, m], raw[:, m, :]).then_inc(dve_setup, 1)
            for m in (1, 4):
                v.tensor_scalar(mods[:, :, m], raw[:, m, :], 1.0, None, ALU.add).then_inc(dve_setup, 1)
            for m in (2, 5):
                v.tensor_copy(mods[:, :, m], raw[:, m, :]).then_inc(dve_setup, 1)
            for n, m in enumerate((2, 5)):
                dve.wait_ge(dve_setup, 9)
                v.tensor_scalar(sign[:, n, :], mods[:, :, m], 0.0, 2.0, ALU.is_ge, ALU.mult).then_inc(dve_setup, 1)
                v.scalar_tensor_tensor(out=size[:, n, :], in0=mods[:, :, m], scalar=-1.0, in1=mods[:, :, m],
                                       op0=ALU.mult, op1=ALU.max).then_inc(dve_setup, 1)
                dve.wait_ge(dve_setup, 11 + 3 * n)
                v.tensor_scalar(size[:, n, :], size[:, n, :], 0.25, None, ALU.max).then_inc(dve_setup, 1)
            dve.wait_ge(dve_setup, 15)
            for n, m in enumerate((2, 5)):
                v.scalar_tensor_tensor(out=mods[:, :, m], in0=sign[:, n, :], scalar=1.0, in1=size[:, n, :],
                                       op0=ALU.subtract, op1=ALU.mult).then_inc(dve_setup, 1)
            dve.wait_ge(dve_setup, 17)
            v.tensor_scalar(mods[:, :, 6], mods[:, :, 2], bo_sb[:, 0:1], None, ALU.mult).then_inc(dve_setup, 1)
            def carry():
                v.memset(idle[:, :], 0.0)

            def layernorm(part, src, st, ag, rs, dst, done, b, per, k0):
                k = k0 + 5

                def step(ins):
                    nonlocal k
                    k += 1
                    ins.then_inc(done, 1)
                    wait(dve, done, b, per, k)
                if part == 0:
                    for n in range(NT):
                        v.bn_stats(st[:, n, :], src[:, n, :]).then_inc(done, 1)
                    wait(dve, done, b, per, k0 + 4)
                    carry()
                    for n in range(NT):
                        ins = v.bn_aggr(ag[:, n, :], st[:, n, :])
                    ins.then_inc(done, 1)
                elif part == 1:
                    wait(dve, done, b, per, k0 + 5)
                    var, a_, b_ = root[:, 0, :], root[:, 1, :], root[:, 2, :]
                    step(v.tensor_scalar(var, ag[:, :, 1], EPS, None, ALU.add))
                    step(v.tensor_scalar(rs[:, :].bitcast(I32), var.bitcast(I32), -0.5, float(0x5F3759DF), ALU.mult, ALU.add))
                    for _ in range(3):
                        step(v.tensor_tensor(a_, rs[:, :], rs[:, :], ALU.mult))
                        step(v.scalar_tensor_tensor(out=b_, in0=a_, scalar=-0.5, in1=var, op0=ALU.mult, op1=ALU.mult))
                        step(v.scalar_tensor_tensor(out=rs[:, :], in0=b_, scalar=1.5, in1=rs[:, :], op0=ALU.add, op1=ALU.mult))
                else:
                    for n in range(NT):
                        v.tensor_scalar(dst[:, n, :], src[:, n, :], ag[:, n, 0:1], rs[:, n:n + 1],
                                        ALU.subtract, ALU.mult).then_inc(done, 1)

            def ln1(b, part):
                if part == 0:
                    wait(dve, x_loaded, b, 16, 16)
                    v.tensor_copy(mod_a[:, b.par, :], mods[:, bass.ds(b.index(), 1), :].rearrange("p b m -> p (b m)")).then_inc(dve_ln1, 1)
                elif part == 2:
                    if b.reg is None and b.const == 1:
                        wait(dve, pe_a, b.plus(-1), PA, 1)
                    elif not (b.reg is None and b.const == 0):
                        wait(dve, pe_c, b.plus(-2), PC, 5)
                        wait(dve, pe_a, b.plus(-1), PA, 1)
                layernorm(part, xt[:, b.par], stats, mv, rstd, xn, dve_ln1, b, LN1, 1)

            def rope(b, k):
                wait(dve, pe_a, b, PA, k + 2)
                if k >= 2:
                    wait(dve, pool_rope, b, 2, 1)
                elif not (b.reg is None and b.const == 0):
                    wait(dve, pool_rope, b.plus(-1), 2, 2)
                v.scalar_tensor_tensor(out=rot[:, k % 2, :], in0=b_proj(b, k + 1), scalar=bqk_sb[:, k:k + 1],
                                       in1=trig_sb[:, k % 2, :], op0=ALU.add, op1=ALU.mult).then_inc(dve_rope, 1)

            def values(b):
                wait(dve, pe_a, b, PA, 7)
                src = b_values.rearrange("p (a r c d) -> p a r c d", r=2, c=4, d=DH)
                dst = vpad[:, :, :, :].rearrange("p n (g r c) w -> p (n g) r c w", r=2, c=4)
                for r in range(2):
                    v.tensor_copy(dst[:, :, r, :, VW * r:VW * r + DH], src[:, :, r, :, :]).then_inc(dve_v, 1)

            def row_max(i, n):
                pair, k = divmod(n, 5)
                wait(dve, pe_rows, i, RT, n + 1)
                h = 2 * pair + (k // 2 if k < 4 else 0)
                tile_ = row_tile(n)
                if k == 4:
                    ins = v.tensor_reduce(mx[:, 1, h:h + 2], tile_.rearrange("p (a c) -> p a c", a=2), AX.X, ALU.max)
                elif k % 2 == 0:
                    ins = v.tensor_reduce(mx[:, 3, h:h + 1], tile_, AX.X, ALU.max)
                else:
                    ins = v.tensor_reduce(mpart[:, h, :], tile_.rearrange("p (a c) -> p a c", a=4), AX.X, ALU.max)
                ins.then_inc(dve_rows, 1)

            def split_max(i):
                wait(dve, dve_rows, i, RT, RT)
                v.tensor_reduce(mx[:, 2, :], mpart[:, :, 0:3], AX.X, ALU.max).then_inc(dve_m, 1)
                v.tensor_copy(mx[:, 0, :], mpart[:, :, 3]).then_inc(dve_m, 1)
                wait(dve, dve_m, i, 6, 2)
                v.tensor_scalar(msplit[:, :, 0, :], mx[:, :, :], -1.0, None, ALU.mult).then_inc(dve_m, 1)
                wait(dve, dve_m, i, 6, 3)
                v.scalar_tensor_tensor(out=mrest[:, :, :], in0=mx[:, :, :], scalar=-1.0, in1=msplit[:, :, 0, :],
                                       op0=ALU.mult, op1=ALU.subtract).then_inc(dve_m, 1)
                wait(dve, dve_m, i, 6, 4)
                v.tensor_copy(msplit[:, :, 1, :], mrest[:, :, :]).then_inc(dve_m, 1)
                wait(dve, dve_m, i, 6, 5)
                v.tensor_tensor(msplit[:, :, 2, :], mrest[:, :, :], msplit[:, :, 1, :], ALU.subtract).then_inc(dve_m, 1)

            def hidden(b, e):
                wait(dve, act_silu, b, NF, e + 1)
                wait(dve, pe_up, b, NF, e + 1)
                if e >= 2:
                    wait(dve, pe_down, b, NF, e - 1)
                v.tensor_tensor(hid[:, (b.const + e) % 2, :], silu[:, (b.const + e) % 2, :], b_up, ALU.mult).then_inc(dve_hid, 1)

            def hT_of(b):
                wait(dve, pe_a, b, PA, 1)
                v.tensor_scalar(hT[:, :], b_proj(b, 0), mod_a[:, b.par, 1:2], mod_a[:, b.par, 0:1],
                                ALU.mult, ALU.add).then_inc(dve_h, 1)

            def mT_of(i):
                wait(dve, pe_mT, i, 1, 1)
                if not (i.reg is None and i.const == 0):
                    wait(dve, m_rows, i.plus(-1), 48, 48)
                v.tensor_copy(mT[:, :], row_tile(0).bitcast(BF16)[0:3 * H, 0:S]).then_inc(dve_mT, 1)

            def copy_attn(i, g, proj):
                wait(dve, pe_pv, i, H, 8 * (g + 1))
                if g == 0 and proj:
                    wait(dve, pool_rope, i.plus(1), 2, 2)
                if g == 0 and not (i.reg is None and i.const == 0):
                    wait(dve, pe_c, i.plus(-1), PC, 1)
                v.tensor_copy(xs[:, g, :], b_attn[g]).then_inc(dve_x, 1)

            def normalise(i):
                wait(dve, pe_c, i, PC, 1)
                for g in range(2):
                    t = banks[:, g, :].rearrange("p (n c w) -> p n c w", n=NT, c=4)
                    den = t[:, :, :, DH:DH + VW + 1:VW]
                    v.reciprocal(rden[:, g], den).then_inc(dve_o, 1)
                wait(dve, dve_o, i, 6, 2)
                for g in range(2):
                    t = banks[:, g, :].rearrange("p (n c w) -> p n c w", n=NT, c=4)
                    for r in range(2):
                        dst = o[:, :, 64 * g + 32 * r:64 * g + 32 * r + 32].rearrange("p n (c d) -> p n c d", d=DH)
                        v.tensor_tensor(dst, t[:, :, :, VW * r:VW * r + DH],
                                        rden[:, g, :, :, r:r + 1].broadcast_to([P, NT, 4, DH]), ALU.mult).then_inc(dve_o, 1)

            def residual(i, part):
                if part == 0:
                    wait(dve, pe_c, i, PC, 4)
                    v.tensor_tensor(x1[:, i.par], xt[:, i.par], banks[:, 0, :].rearrange("p (n e) -> p n e", n=NT),
                                    ALU.add).then_inc(dve_ln2, 1)
                    v.tensor_copy(gate_b[:, i.par, :], gate_rows[:, bass.ds(i.index(), 1), :].rearrange("p b e -> p (b e)")).then_inc(dve_ln2, 1)
                    wait(dve, dve_ln2, i, LN2, 2)
                layernorm(part, x1[:, i.par], stats2, mv2, rstd2, xn, dve_ln2, i, LN2, 2)

            def high_bits(i):
                wait(dve, act_c, i, AC, 3)
                if not (i.reg is None and i.const == 0):
                    wait(dve, pool_low, i.plus(-1), 1, 1)
                v.tensor_scalar(h2bits[:, :], h2T[:, :].bitcast(U32), HIGH_BITS, None, ALU.bitwise_and).then_inc(dve_bits, 1)

            def routing(i):
                k = [0]

                def step(ins, last=True, carried=False):
                    k[0] += 1
                    ins.then_inc(dve_g, 1)
                    if last:
                        wait(dve, dve_g, i, DG, k[0])
                    if carried:
                        carry()
                wait(dve, act_c, i, AC, 5)
                step(v.tensor_scalar(eg1[:, :, :], eg[:, :, :], 1.0, None, ALU.add))
                step(v.reciprocal(score[:, :, :], eg1[:, :, :]))
                step(v.tensor_tensor(pick[:, :, :], score[:, :, :], ebias_sb[:, :, :], ALU.add), carried=True)
                for n in range(NT):
                    step(v.max(top[:, n, :], pick[:, n, :]), n == NT - 1, n == NT - 1)
                for n in range(NT):
                    step(v.match_replace(left[:, n, :], top[:, n, :], pick[:, n, :], NEG), n == NT - 1)
                step(v.scalar_tensor_tensor(out=chosen[:, :, :], in0=left[:, :, :], scalar=NEG, in1=score[:, :, :],
                                            op0=ALU.is_equal, op1=ALU.mult))
                step(v.tensor_reduce(total[:, :], chosen[:, :, :], AX.X, ALU.add))
                step(v.reciprocal(rtotal[:, :], total[:, :]))
                step(v.scalar_tensor_tensor(out=comb[:, i.par, :, :], in0=chosen[:, :, :], scalar=ROUTE_SCALE,
                                            in1=rtotal[:, :].rearrange("p (n a) -> p n a", a=1).broadcast_to([P, NT, NE]),
                                            op0=ALU.mult, op1=ALU.mult), False)
                assert k[0] == DG

            def stage(i, ffn, proj):
                prev, nxt = i.plus(-1), i.plus(1)
                for s in range(E_SLOT1):
                    rows = [ROW_TILES * ROW_STEPS.index(s) + k for k in range(ROW_TILES)] if s in ROW_STEPS else []
                    for n in rows[:3]:
                        row_max(i, n)
                    if ffn:
                        hidden(prev, s)
                    for n in rows[3:]:
                        row_max(i, n)
                    if s == ROW_STEPS[-1]:
                        split_max(i)
                    if s == ROW_STEPS[-1] + 1:
                        mT_of(i)
                    if proj and s in LN1_AT:
                        ln1(nxt, LN1_AT[s])
                if proj:
                    hT_of(nxt)
                    for k in range(4):
                        rope(nxt, k)
                copy_attn(i, 0, proj)
                copy_attn(i, 1, proj)
                if proj:
                    values(nxt)
                normalise(i)
                if ffn:
                    for e in (11, 12, 13):
                        hidden(prev, e)
                residual(i, 0)
                if ffn:
                    hidden(prev, 14)
                residual(i, 1)
                residual(i, 2)
                if ffn:
                    hidden(prev, 15)
                high_bits(i)
                if ffn:
                    hidden(prev, 16)
                routing(i)

            dve.wait_ge(mod_loaded, 16 * len(mod_loads))
            dve.wait_ge(dve_setup, 18)
            for part in range(3):
                ln1(Batch(0), part)
            dve.wait_ge(w_loaded, 16 * len(loads))
            v.tensor_copy(identb[:, :], ident_sb[:, :]).then_inc(dve_setup, 1)
            hT_of(Batch(0))
            for k in range(4):
                rope(Batch(0), k)
            dve.wait_ge(act_gelu, 2)
            rest_k = yo[:, :, :].rearrange("p n e -> p (n e)")
            v.tensor_copy(parts[:, 1, 0, :], qk[:, 1, :]).then_inc(k_split, 1)
            dve.wait_ge(k_split, 1)
            v.tensor_tensor(rest_k, qk[:, 1, :], parts[:, 1, 0, :], ALU.subtract).then_inc(k_split, 1)
            dve.wait_ge(k_split, 2)
            v.tensor_copy(parts[:, 1, 1, :], rest_k).then_inc(k_split, 1)
            dve.wait_ge(k_split, 3)
            v.tensor_tensor(parts[:, 1, 2, :], rest_k, parts[:, 1, 1, :], ALU.subtract).then_inc(k_split, 1)
            dve.wait_ge(pool_setup, 6)
            values(Batch(0))
            diag = ye[:, :, :].rearrange("p a c -> p (a c)").rearrange("p (b e) -> p b e", e=E)
            for b in range(B):
                v.tensor_scalar(diag[:, b, :], ident_sb[:, :], mods[:, b, 5:6], None, ALU.mult).then_inc(dve_diag, 1)
            dve.wait_ge(late_loaded, 16 * len(late_loads))
            dve.wait_ge(ffn_loaded, 16 * len(ffn_loads))
            for m in range(2):
                v.tensor_scalar(staged[:, 2 + m].bitcast(U32), staged[:, m].bitcast(U32), HIGH_BITS, None,
                                ALU.bitwise_and).then_inc(dve_wsplit, 1)
            dve.wait_ge(dve_wsplit, 2)
            for m, dst in enumerate((wg_lo, wu_lo)):
                v.tensor_tensor(dst[:, :, :], staged[:, m], staged[:, 2 + m], ALU.subtract).then_inc(dve_wsplit, 1)
            schedule(dve, stage)
            for e in range(NF):
                hidden(Batch(B - 1), e)

        @block.tensor
        def _(pe):
            mm = nc.tensor.matmul
            pe.wait_ge(act_setup, 1)
            for m in range(6):
                last = mm(banks[:, 0, B * m:B * m + B], wmod_sb[:, m, :], cs_sb[:, :], start=True, stop=True)
            last.then_inc(pe_setup, 1)

            def project(b, k):
                if k == 0:
                    wait(pe, dve_ln1, b, LN1, LN1)
                    for n in range(NT):
                        last = nc.tensor.transpose(b_proj(b, 0)[:, n * P:(n + 1) * P], xn[:, n, :], ident_sb[:, :])
                elif k < 5:
                    if k == 1:
                        wait(pe, dve_h, b, 1, 1)
                    elif not (b.reg is None and b.const == 0):
                        wait(pe, dve_rope, b, 4, k - 1)
                    last = mm(b_proj(b, k), wqkv_sb[:, k - 1, :], hT[:, :], start=True, stop=True)
                elif k == 5:
                    if not (b.reg is None and b.const == 0):
                        wait(pe, dve_rope, b, 4, 4)
                    last = mm(b_proj(b, 5)[0:DC, :], wkv_sb[:, :], hT[:, :], start=True, stop=True)
                else:
                    wait(pe, act_gelu, b, 3, 3)
                    for n in range(NT):
                        last = mm(b_values[:, n * P:(n + 1) * P], ckv[:, n * P:(n + 1) * P], wv_sb[:, :],
                                  start=True, stop=True)
                last.then_inc(pe_a, 1)

            def diagonal_rows(dst):
                return mm(dst, identb[:, :], mask_sb[:, :], start=False, stop=True, skip_group_check=True)

            def diagonal_cols(dst):
                return mm(dst, mask_sb[:, :], identb[:, :], start=False, stop=True, skip_group_check=True)

            def rows(i, h, n, dst, at):
                w = P * (n + 1)
                mm(dst[:, at:at + w], qs[:, h, n * P:(n + 1) * P], ks[:, h, 0:w],
                   start=True, stop=False, skip_group_check=True)
                return diagonal_rows(dst[:, at + w - P:at + w])

            def row_scores(i, n):
                pair, k = divmod(n, 5)
                if n >= 4:
                    wait(pe, dve_rows, i, RT, n - 3)
                h = 2 * pair + (k // 2 if k < 4 else 0)
                dst = row_tile(n)
                if k == 4:
                    rows(i, h, 1, dst, 0)
                    last = rows(i, h + 1, 1, dst, 256)
                elif k % 2 == 0:
                    last = rows(i, h, 3, dst, 0)
                else:
                    rows(i, h, 2, dst, 0)
                    last = rows(i, h, 0, dst, 384)
                last.then_inc(pe_rows, 1)

            def turn_max(i):
                wait(pe, dve_m, i, 6, 6)
                t = row_tile(0).bitcast(BF16)
                for n in range(NT):
                    last = nc.tensor.transpose(t[:, n * P:(n + 1) * P],
                                               msplit[:, n, :, :].rearrange("p s h -> p (s h)"), identb[:, :])
                last.then_inc(pe_mT, 1)

            def cols(i, h, j, dst):
                mm(dst, ks[:, h, j * P:(j + 1) * P], qs[:, h, j * P:S],
                   start=True, stop=False, skip_group_check=True)
                return diagonal_cols(dst[:, 0:P])

            def col_scores(i, h):
                n = 3 * (h // 2) + h % 2
                if h >= 2:
                    wait(pe, act_exp, i, CT, n - 2)
                dst = col_pair(h)
                cols(i, h, 0, dst[:, 0, :])
                cols(i, h, 1, dst[:, 1, 0:384])
                cols(i, h, 3, dst[:, 1, 384:512]).then_inc(pe_cols, 1)
                if h % 2:
                    if h >= 3:
                        wait(pe, act_exp, i, CT, 3 * (h // 2))
                    cols(i, h - 1, 2, col_shared[:, 0:256])
                    cols(i, h, 2, col_shared[:, 256:512]).then_inc(pe_cols, 1)

            def attend(i, turn, proj):
                quad, t = divmod(turn, NT)
                j = KEY_ORDER[t]
                g, r = divmod(quad, 2)
                if t == 0:
                    wait(pe, act_exp, i, CT, 6 * quad + 5)
                    if quad == 2 and proj:
                        wait(pe, act_gelu, i.plus(1), 3, 3)
                if t == NT - 1:
                    wait(pe, act_exp, i, CT, 6 * quad + 6)
                for c in range(4):
                    h = 4 * quad + c
                    at = P_AT[j]
                    last = mm(b_attn[g][32 * c:32 * c + 32, j * P:S], vpad[:, j, h, :],
                              probs[:, h % 8, at:at + S - j * P], start=(r == 0 and t == 0),
                              stop=(r == 1 and t == NT - 1), skip_group_check=True, tile_position=(0, 32 * c))
                last.then_inc(pe_pv, 1)

            def three_passes(dst, w_hi, w_lo, b, e):
                mm(dst, w_hi[:, e, :], h2_hi[:, b.par, :], start=True, stop=False)
                if dst is b_gate and e == 0:
                    wait(pe, pool_low, b, 1, 1)
                mm(dst, w_hi[:, e, :], h2_lo[:, b.par, :], start=False, stop=False)
                return mm(dst, w_lo[:, e, :], h2_hi[:, b.par, :], start=False, stop=True)

            def expert_in(b, e, what):
                if what == "gate":
                    if e:
                        wait(pe, act_silu, b, NF, e)
                    if e == E_SLOT1 and not (b.reg is None and b.const == B - 1):
                        wait(pe, dve_x, b.plus(1), 2, 1)
                    if e == 0:
                        wait(pe, act_c, b, AC, 4)
                    three_passes(b_gate, wg_hi, wg_lo, b, e).then_inc(pe_gate, 1)
                else:
                    if e:
                        wait(pe, dve_hid, b, NF, e)
                    three_passes(b_up, wu_hi, wu_lo, b, e).then_inc(pe_up, 1)

            def expert_down(b, e):
                wait(pe, dve_hid, b, NF, e + 1)
                if e:
                    wait(pe, act_ye, b, NF, e)
                for n in range(NT):
                    last = mm(b_y[:, n * P:(n + 1) * P], hid[:, (b.const + e) % 2, n * P:(n + 1) * P], wd_sb[:, e, :],
                              start=True, stop=True)
                last.then_inc(pe_down, 1)

            def back(src, dst, w):
                for n in range(NT):
                    last = nc.tensor.transpose(dst[:, n * P:(n + 1) * P], src(n), w)
                return last

            def chain(i, k):
                if k == 1:
                    wait(pe, dve_x, i, 2, 2)
                    for g in range(2):
                        last = back(lambda n: xs[:, g, n * P:(n + 1) * P], banks[:, g, :], ident_sb[:, :])
                elif k == 2:
                    wait(pe, dve_o, i, 6, 6)
                    last = back(lambda n: o[:, n, :], banks[:, 2, :], ident_sb[:, :])
                elif k == 3:
                    wait(pe, act_c, i, AC, 1)
                    last = mm(banks[:, 3, :], wo_sb[:, :], oT[:, :], start=True, stop=True)
                elif k == 4:
                    wait(pe, act_c, i, AC, 2)
                    last = back(lambda n: aT[:, n * P:(n + 1) * P], banks[:, 0, :], ident_sb[:, :])
                elif k == 5:
                    wait(pe, dve_ln2, i, LN2, LN2)
                    last = back(lambda n: xn[:, n, :], banks[:, 1, :], ident_sb[:, :])
                else:
                    wait(pe, act_c, i, AC, 3)
                    for n in range(NT):
                        last = mm(banks[:, 2, n * NE:(n + 1) * NE], h2T[:, n * P:(n + 1) * P], gate_sb[:, :],
                                  start=True, stop=True)
                last.then_inc(pe_c, 1)

            def stage(i, ffn, proj):
                prev, nxt = i.plus(-1), i.plus(1)
                wait(pe, stacks, i, ST, ST)
                for s in range(E_SLOT1):
                    def row(k):
                        if s in ROW_STEPS:
                            if ffn and s == ROW_STEPS[0] and k == 2:
                                wait(pe, act_c, prev, AC, 5)
                            row_scores(i, ROW_TILES * ROW_STEPS.index(s) + k)
                    row(0)
                    row(1)
                    if ffn:
                        expert_in(prev, s, "gate")
                    row(2)
                    if ffn:
                        expert_in(prev, s, "up")
                    row(3)
                    if s == ROW_STEPS[-1] + 1:
                        turn_max(i)
                    if ffn and s:
                        expert_down(prev, s - 1)
                    row(4)
                wait(pe, m_rows, i, 48, 48)
                for h in range(H):
                    if ffn and h == 1:
                        wait(pe, dve_hid, prev, NF, E_SLOT1)
                    col_scores(i, h)
                    if proj and h == 1:
                        project(nxt, 0)
                    if proj and 3 <= h <= 7:
                        project(nxt, h - 2)
                    for turn in ATTEND_AT.get(h, ()):
                        attend(i, turn, proj)
                    if ffn and h == GELU_AT + 2:
                        expert_down(prev, 10)
                attend(i, 11, proj)
                for turn in range(H - NT, H):
                    attend(i, turn, proj)
                if proj:
                    project(nxt, 6)
                if ffn:
                    expert_in(prev, 11, "gate")
                chain(i, 1)
                if ffn:
                    expert_in(prev, 11, "up")
                    expert_in(prev, 12, "gate")
                chain(i, 2)
                if ffn:
                    expert_down(prev, 11)
                    expert_in(prev, 12, "up")
                if proj:
                    wait(pe, dve_v, nxt, 2, 2)
                chain(i, 3)
                if ffn:
                    expert_in(prev, 13, "gate")
                    expert_down(prev, 12)
                    expert_in(prev, 13, "up")
                chain(i, 4)
                if ffn:
                    expert_in(prev, 14, "gate")
                    expert_down(prev, 13)
                    expert_in(prev, 14, "up")
                    expert_in(prev, 15, "gate")
                    expert_down(prev, 14)
                    expert_in(prev, 15, "up")
                    expert_in(prev, 16, "gate")
                chain(i, 5)
                if ffn:
                    expert_down(prev, 15)
                    expert_in(prev, 16, "up")
                chain(i, 6)
                if ffn:
                    expert_down(prev, 16)
                elif proj:
                    pe.wait_ge(ffn_loaded, 16 * len(ffn_loads))
                    pe.wait_ge(act_wsplit, 2)
                    pe.wait_ge(dve_wsplit, 4)

            pe.wait_ge(w_loaded, 16 * len(loads))
            for k in range(7):
                project(Batch(0), k)
            pe.wait_ge(dve_setup, 19)
            pe.wait_ge(dve_diag, B)
            for n in range(2):
                last = mm(banks[:, 1 + n, :], y_sum[:, 0:P], ye[:, n, :], start=True, stop=True)
            last.then_inc(pe_rows_b, 1)
            pe.wait_ge(act_rows_b, 2)
            pe.wait_ge(dve_v, 2)
            pe.wait_ge(stored, 16)
            pe.wait_ge(late_loaded, 16 * len(late_loads))
            schedule(pe, stage)
            last = Batch(B - 1)
            for e in range(NF):
                expert_in(last, e, "gate")
                expert_in(last, e, "up")
                if e:
                    expert_down(last, e - 1)
            expert_down(last, NF - 1)


def constants():
    import numpy as np

    def bf16_bits(a):
        return (np.ascontiguousarray(a, np.float32).view(np.uint32) >> 16).astype(np.uint16)
    inv = (1.0 / 10000.0 ** (np.arange(0, E, 2, dtype=np.float32) / np.float32(E))).astype(np.float32)
    freqs = np.arange(S, dtype=np.float32)[None, :] * inv[:, None]
    emb = np.concatenate([freqs, freqs], axis=0)
    signed = np.where(np.arange(E)[:, None] < E // 2, -1.0, 1.0).astype(np.float32)
    trig = np.stack([np.cos(emb), np.sin(emb) * signed], axis=1).astype(np.float32)
    ident = np.eye(P, dtype=np.float32)
    mask = np.where(np.arange(P)[None, :] > np.arange(P)[:, None], NEG, 0.0)
    return trig, ident, bf16_bits(mask)


def kernel(**inputs):
    import numpy as np
    import concourse.bacc as bacc
    from concourse.bass_utils import run_bass_kernel_spmd

    a = {k.removeprefix("L0_"): np.asarray(v) for k, v in inputs.items()}
    trig, ident, mask = constants()
    half = np.r_[E // 2:E, 0:E // 2]
    wq, wk, bq, bk = a["attn_wqr"], a["attn_wkr"], a["attn_bqr"], a["attn_bkr"]

    def stacked(routed, shared):
        return np.concatenate([routed, shared[None]], 0).transpose(2, 0, 1)

    arrays = {
        "x": a["attn_x"],
        "cT": a["c"].T,
        "wmod": a["wmod"].reshape(E, 6, E),
        "wqkv": np.stack([wq, wq[:, half], wk, wk[:, half]], 1),
        "bqk": np.stack([bq, bq[half], bk, bk[half]], 1),
        "wkv": a["attn_wkv"],
        "bkv": a["attn_bkv"][:, None],
        "wv": np.concatenate([a["attn_wv"], a["attn_bv"][None]], 0),
        "wo": a["attn_wo"],
        "bo": a["attn_bo"][:, None],
        "trig": trig,
        "gate": a["ffn_gate_w"].T,
        "ebias": np.broadcast_to(a["ffn_expert_bias"], (P, NT, NE)),
        "wg": stacked(a["ffn_w_gate"], a["ffn_shared_gate_w"]),
        "wu": stacked(a["ffn_w_up"], a["ffn_shared_up_w"]),
        "wd": stacked(a["ffn_w_down"], a["ffn_shared_down_w"]),
        "ident": ident,
        "mask": mask,
    }
    nc = bacc.Bacc("TRN2", target_bir_lowering=False, num_devices=1)
    arrays = {f"in_{k}": np.ascontiguousarray(v) for k, v in arrays.items()}
    args = [nc.dram_tensor(k, v.shape, mybir.dt.from_np(v.dtype), kind="ExternalInput").ap() for k, v in arrays.items()]
    out = nc.dram_tensor("out_x", (B, S, E), F32, kind="ExternalOutput").ap()
    scratch = nc.dram_tensor("scratch_parts", (2, 2, P, 3, S), BF16, kind="Internal").ap()
    adaln_block(nc, *args, out, scratch)
    r = run_bass_kernel_spmd(nc, [arrays], core_ids=[0])
    return r.results[0]["out_x"]
```
